# Optimizing a Trainium2 kernel written in Bass

```python
import numpy as np
import jax
import jax.numpy as jnp

def _softmax(x, axis=-1):
    return jax.nn.softmax(x, axis=axis)

def _gelu(x):
    return jax.nn.gelu(x, approximate=True)

def _silu(x):
    return jax.nn.silu(x)

def _sigmoid(x):
    return jax.nn.sigmoid(x)

def _layernorm(x, axis=-1, eps=1e-05):
    m = jnp.mean(x, axis=axis, keepdims=True)
    v = jnp.var(x, axis=axis, keepdims=True)
    return (x - m) / jnp.sqrt(v + eps)

def _scatter_add(tgt, idx, src, axis=0):
    return tgt.at[idx].add(src)

def _segment_sum(src, seg, n):
    return jax.ops.segment_sum(src, seg, n)
kernel_name = 'mk_rec_standalone_d1_rec_r8_6785fb'

def setup_inputs(seed: int=0):
    np.random.seed(seed)
    _w = jnp.asarray

    def _rec_inputs():
        import jax
        import jax.numpy as jnp
        _rk = jax.random.key(seed)
        r_x_dense = -0.000692196 + 0.998807 * jax.random.normal(jax.random.fold_in(_rk, 1), (512, 13), jnp.float32)
        r_x_sparse = jnp.stack([jax.random.randint(jax.random.fold_in(jax.random.fold_in(_rk, 2), 0), (512,), 0, 99999, jnp.int32), jax.random.randint(jax.random.fold_in(jax.random.fold_in(_rk, 2), 1), (512,), 0, 12499, jnp.int32), jax.random.randint(jax.random.fold_in(jax.random.fold_in(_rk, 2), 2), (512,), 4, 99997, jnp.int32), jax.random.randint(jax.random.fold_in(jax.random.fold_in(_rk, 2), 3), (512,), 2, 99997, jnp.int32), jax.random.randint(jax.random.fold_in(jax.random.fold_in(_rk, 2), 4), (512,), 1, 99988, jnp.int32), jax.random.randint(jax.random.fold_in(jax.random.fold_in(_rk, 2), 5), (512,), 1, 99996, jnp.int32), jax.random.randint(jax.random.fold_in(jax.random.fold_in(_rk, 2), 6), (512,), 12, 99997, jnp.int32), jax.random.randint(jax.random.fold_in(jax.random.fold_in(_rk, 2), 7), (512,), 17, 99995, jnp.int32), jax.random.randint(jax.random.fold_in(jax.random.fold_in(_rk, 2), 8), (512,), 0, 99998, jnp.int32), jax.random.randint(jax.random.fold_in(jax.random.fold_in(_rk, 2), 9), (512,), 0, 99998, jnp.int32), jax.random.randint(jax.random.fold_in(jax.random.fold_in(_rk, 2), 10), (512,), 3, 99993, jnp.int32), jax.random.randint(jax.random.fold_in(jax.random.fold_in(_rk, 2), 11), (512,), 0, 99993, jnp.int32), jax.random.randint(jax.random.fold_in(jax.random.fold_in(_rk, 2), 12), (512,), 1, 99988, jnp.int32), jax.random.randint(jax.random.fold_in(jax.random.fold_in(_rk, 2), 13), (512,), 0, 99997, jnp.int32), jax.random.randint(jax.random.fold_in(jax.random.fold_in(_rk, 2), 14), (512,), 3, 99993, jnp.int32), jax.random.randint(jax.random.fold_in(jax.random.fold_in(_rk, 2), 15), (512,), 10, 99994, jnp.int32), jax.random.randint(jax.random.fold_in(jax.random.fold_in(_rk, 2), 16), (512,), 10, 99998, jnp.int32), jax.random.randint(jax.random.fold_in(jax.random.fold_in(_rk, 2), 17), (512,), 18, 99979, jnp.int32), jax.random.randint(jax.random.fold_in(jax.random.fold_in(_rk, 2), 18), (512,), 1, 99996, jnp.int32), jax.random.randint(jax.random.fold_in(jax.random.fold_in(_rk, 2), 19), (512,), 6, 99987, jnp.int32), jax.random.randint(jax.random.fold_in(jax.random.fold_in(_rk, 2), 20), (512,), 6, 12500, jnp.int32), jax.random.randint(jax.random.fold_in(jax.random.fold_in(_rk, 2), 21), (512,), 2, 12500, jnp.int32), jax.random.randint(jax.random.fold_in(jax.random.fold_in(_rk, 2), 22), (512,), 7, 12498, jnp.int32), jax.random.randint(jax.random.fold_in(jax.random.fold_in(_rk, 2), 23), (512,), 2, 99999, jnp.int32), jax.random.randint(jax.random.fold_in(jax.random.fold_in(_rk, 2), 24), (512,), 29, 99990, jnp.int32), jax.random.randint(jax.random.fold_in(jax.random.fold_in(_rk, 2), 25), (512,), 10, 99986, jnp.int32)], axis=1)
        return (r_x_dense, r_x_sparse)
    r_x_dense, r_x_sparse = _rec_inputs()

    def _L0_rec_setup():
        import jax, jax.numpy as jnp
        import numpy as np
        F = 26
        V = 12500
        D = 32
        DENSE = 13
        HID = (1024, 512, 256)
        B = 2048
        key = jax.random.key(seed)
        ks = jax.random.split(key, 16)
        x_sparse = jax.random.randint(ks[0], (B, F), 0, V, dtype=jnp.int32)
        x_dense = jax.random.normal(ks[1], (B, DENSE), dtype=jnp.float32)
        emb_tables = jax.random.normal(ks[2], (F, V, D), dtype=jnp.float32) * 0.05
        lin_tables = jax.random.normal(ks[3], (F, V), dtype=jnp.float32) * 0.05
        dnn_in = F * D + DENSE
        dims = (dnn_in,) + HID
        params = {}
        for i in range(len(HID)):
            params[f'W{i}'] = jax.random.normal(ks[4 + i], (dims[i], dims[i + 1]), dtype=jnp.float32) * (1.0 / np.sqrt(dims[i]))
            params[f'b{i}'] = jnp.zeros((dims[i + 1],), dtype=jnp.float32)
        Wout = jax.random.normal(ks[10], (HID[-1], 1), dtype=jnp.float32) * (1.0 / np.sqrt(HID[-1]))
        bout = jnp.zeros((1,), dtype=jnp.float32)
        return dict(x_sparse=x_sparse, x_dense=x_dense, emb_tables=emb_tables, lin_tables=lin_tables, W0=params['W0'], b0=params['b0'], W1=params['W1'], b1=params['b1'], W2=params['W2'], b2=params['b2'], Wout=Wout, bout=bout)
    _L0_rec_all = _L0_rec_setup()
    _L0_rec_in = {k: v for k, v in _L0_rec_all.items() if k in ('emb_tables', 'lin_tables', 'W0', 'b0', 'W1', 'b1', 'W2', 'b2', 'Wout', 'bout')}
    del _L0_rec_all
    return {'r_x_dense': r_x_dense, 'r_x_sparse': r_x_sparse, 'L0_rec_emb_tables': _L0_rec_in['emb_tables'], 'L0_rec_lin_tables': _L0_rec_in['lin_tables'], 'L0_rec_W0': _L0_rec_in['W0'], 'L0_rec_b0': _L0_rec_in['b0'], 'L0_rec_W1': _L0_rec_in['W1'], 'L0_rec_b1': _L0_rec_in['b1'], 'L0_rec_W2': _L0_rec_in['W2'], 'L0_rec_b2': _L0_rec_in['b2'], 'L0_rec_Wout': _L0_rec_in['Wout'], 'L0_rec_bout': _L0_rec_in['bout']}

def reference(r_x_dense, r_x_sparse, L0_rec_emb_tables, L0_rec_lin_tables, L0_rec_W0, L0_rec_b0, L0_rec_W1, L0_rec_b1, L0_rec_W2, L0_rec_b2, L0_rec_Wout, L0_rec_bout):
    import jax
    import jax.numpy as jnp

    def _L0_rec_ref(x_sparse, x_dense, emb_tables, lin_tables, W0, b0, W1, b1, W2, b2, Wout, bout):
        import jax, jax.numpy as jnp
        import numpy as np
        F = 26
        V = 12500
        D = 32
        DENSE = 13
        HID = (1024, 512, 256)
        B = 2048
        f_idx = jnp.arange(F)[None, :]
        emb = emb_tables[f_idx, x_sparse]
        lin = lin_tables[f_idx, x_sparse]
        linear_logit = lin.sum(axis=1)
        s = emb.sum(axis=1)
        fm_logit = 0.5 * ((s * s).sum(axis=-1) - (emb * emb).sum(axis=(1, 2)))
        h = jnp.concatenate([emb.reshape(emb.shape[0], F * D), x_dense], axis=1)
        h = jax.nn.relu(h @ W0 + b0)
        h = jax.nn.relu(h @ W1 + b1)
        h = jax.nn.relu(h @ W2 + b2)
        dnn_logit = (h @ Wout + bout)[:, 0]
        return jax.nn.sigmoid(linear_logit + fm_logit + dnn_logit)
    y = _L0_rec_ref(r_x_sparse, r_x_dense, L0_rec_emb_tables, L0_rec_lin_tables, L0_rec_W0, L0_rec_b0, L0_rec_W1, L0_rec_b1, L0_rec_W2, L0_rec_b2, L0_rec_Wout, L0_rec_bout)
    return y

_drawn_inputs = setup_inputs


def setup_inputs(seed=0):
    import zlib

    import numpy as np

    out = dict(_drawn_inputs(seed))
    spreads = {'L0_rec_b0': (0.0, 0.766), 'L0_rec_b1': (0.0, 0.636), 'L0_rec_b2': (0.0, 0.272)}
    factors = {}
    for name, (base, spread) in spreads.items():
        noise = np.random.default_rng([zlib.crc32(name.encode()), seed]).standard_normal(out[name].shape)
        drawn = base * np.exp(spread * noise) if base else spread * noise
        out[name] = jnp.asarray(drawn.astype(out[name].dtype))
    for name, factor in factors.items():
        out[name] = (out[name] * factor).astype(out[name].dtype)
    return out
```

```python
from contextlib import ExitStack

import concourse.bass as bass
from concourse import mybir

ALU = mybir.AluOpType
ACT = mybir.ActivationFunctionType
AX = mybir.AxisListType
F32 = mybir.dt.float32
I32 = mybir.dt.int32

P = 128
BLOCK = 32
BANK = 512
LOOPED_BLOCKS = 4
LAST_GROUPS = (2, 2)


def deepfm(nc, table, slots, w0, w1, w2, dense_t, columns, out):
    rows, ROW = table.shape
    D = ROW - 1
    BATCH = out.shape[0]
    DENSE = dense_t.shape[0]
    IN, H1 = w0.shape
    H2, H3 = w2.shape
    FEATURES = (IN - DENSE) // D
    VOCAB = rows // FEATURES
    PER_QUAD = P // BLOCK
    QUADS = FEATURES // PER_QUAD
    TAIL = IN - QUADS * P
    PAIR = TAIL - DENSE
    assert D == BLOCK and PAIR == P // 2
    BLOCKS = BATCH // BLOCK
    UNIT = 2 * QUADS + 1
    GATHERS = BLOCKS // 2 * UNIT
    GROUP_IDS = LOOPED_BLOCKS // 2 * UNIT
    M1, M2, M3 = H1 // P, H2 // P, H3 // P
    SLICES = QUADS + 1
    ORDER = [QUADS] + list(range(QUADS))
    LOOPS = (BLOCKS - sum(LAST_GROUPS)) // LOOPED_BLOCKS
    WIDTH = LOOPED_BLOCKS * BLOCK
    W1_PIECES = 4
    B0, B1, B2 = 0, M1, M1 + M2
    WOUT = B2 + M3
    BOUT = WOUT + M3
    SEL = BOUT + 1
    COLUMNS = columns.shape[1]

    def peeled():
        first, number = LOOPS * LOOPED_BLOCKS, LOOPS
        for blocks in LAST_GROUPS:
            yield first, blocks, number
            first, number = first + blocks, number + 1

    def arrived(slice_, first, blocks):
        return (first + blocks) * 8 if slice_ == QUADS else (first + blocks) * 16

    with ExitStack() as ctx:
        def sb(name, shape, dt=F32):
            return ctx.enter_context(nc.sbuf_tensor(name, shape, dt))

        def ps(name, shape):
            return ctx.enter_context(nc.psum_tensor(name, shape, F32))

        def sem(name):
            return ctx.enter_context(nc.semaphore(name))

        slot = sb("slot", [P, 2 * GATHERS], I32)
        wrap = sb("wrap", [P, GATHERS])
        wrapped = sb("wrapped", [P, GATHERS])
        clamped = sb("clamped", [P, GATHERS])
        row_id = sb("row_id", [P, GATHERS], I32)
        group_id = sb("group_id", [P, GROUP_IDS], I32)
        quad_rows = sb("quad_rows", [P, QUADS, LOOPED_BLOCKS, ROW])
        pair_rows = sb("pair_rows", [P, LOOPED_BLOCKS // 2, ROW])
        dense = sb("dense", [P, BATCH])
        x_t = sb("x_t", [P, SLICES, WIDTH])
        w0_sb = sb("w0_sb", [P, SLICES, H1])
        w1_sb = sb("w1_sb", [P, M1, H2])
        w2_sb = sb("w2_sb", [P, M2, H3])
        col = sb("col", [P, COLUMNS])
        weight = sb("weight", [P, 2])
        warm = sb("warm", [1, 1])
        h1 = sb("h1", [P, M1, WIDTH])
        h2 = sb("h2", [P, M2, WIDTH])
        h3 = sb("h3", [P, M3, WIDTH])
        lin = sb("lin", [P, QUADS, LOOPED_BLOCKS])
        pair_lin = sb("pair_lin", [P, LOOPED_BLOCKS // 2])
        lin_sum = sb("lin_sum", [P, LOOPED_BLOCKS])
        x_sq = sb("x_sq", [P, SLICES, WIDTH])
        emb_sum = sb("emb_sum", [P, WIDTH])
        sq_sum = sb("sq_sum", [P, WIDTH])
        s_sq = sb("s_sq", [P, WIDTH])
        probs = sb("probs", [1, BATCH])

        ps1 = ps("ps1", [P, M1 // 2, 2, BANK // 2])
        ps2 = ps("ps2", [P, M2 // 2, 2, BANK // 2])
        ps3 = ps("ps3", [P, M3 // 2, 2, BANK // 2])
        ps_row = ps("ps_row", [P, 2, BANK // 2])
        ps_s, ps_logit = ps_row[:, 0, :], ps_row[0:1, 1, :]

        slot_loaded = sem("slot_loaded")
        col_loaded = sem("col_loaded")
        dense_loaded = sem("dense_loaded")
        w0_loaded = [sem(f"w0_loaded{k}") for k in range(SLICES)]
        w1_loaded = [sem(f"w1_loaded{k}") for k in range(W1_PIECES)]
        w2_loaded = sem("w2_loaded")
        warm_set = sem("warm_set")
        weight_set = sem("weight_set")
        id_step = sem("id_step")
        row_id_ready = sem("row_id_ready")
        ids_ready = [sem(f"ids_ready{k}") for k in range(SLICES)]
        may_gather = sem("may_gather")
        gathered = [sem(f"gathered{k}") for k in range(SLICES)]
        x_ready = sem("x_ready")
        l0_done = sem("l0_done")
        h1_ready = sem("h1_ready")
        l1_done = sem("l1_done")
        h2_ready = sem("h2_ready")
        l2_done = sem("l2_done")
        h3_ready = sem("h3_ready")
        taken = sem("taken")
        sum_step = sem("sum_step")
        squares_ready = sem("squares_ready")
        emb_sum_ready = sem("emb_sum_ready")
        lin_ready = sem("lin_ready")
        sq_sum_ready = sem("sq_sum_ready")
        s_done = sem("s_done")
        s_sq_ready = sem("s_sq_ready")
        logit_done = sem("logit_done")
        probs_ready = sem("probs_ready")
        stored = sem("stored")

        block = ctx.enter_context(nc.Block())

        @block.sync
        def _(sp):
            sp.dma_start(slot[:], slots).then_inc(slot_loaded, 16)
            sp.dma_start(dense[PAIR:TAIL, :], dense_t).then_inc(dense_loaded, 16)
            sp.dma_start(w0_sb[0:TAIL, QUADS, :], w0[QUADS * P:IN, :]).then_inc(w0_loaded[QUADS], 16)
            sp.dma_start(col[:], columns).then_inc(col_loaded, 16)
            for i, k in enumerate(ORDER[1:]):
                if i:
                    before = ORDER[i - 1]
                    sp.wait_ge(gathered[before], arrived(before, 0, LOOPED_BLOCKS))
                sp.dma_start(w0_sb[:, k, :], w0[k * P:k * P + P, :]).then_inc(w0_loaded[k], 16)
            w1_rows = w1.rearrange("(m p) n -> p m n", p=P)
            for piece in range(W1_PIECES):
                if piece < 2:
                    before = ORDER[SLICES - 2 + piece]
                    sp.wait_ge(gathered[before], arrived(before, 0, LOOPED_BLOCKS))
                else:
                    before = ORDER[piece - 2]
                    sp.wait_ge(gathered[before], arrived(before, LOOPED_BLOCKS, LOOPED_BLOCKS))
                some = slice(piece * M1 // W1_PIECES, (piece + 1) * M1 // W1_PIECES)
                sp.dma_start(w1_sb[:, some, :], w1_rows[:, some, :]).then_inc(w1_loaded[piece], 16)
            sp.dma_start(w2_sb[:], w2.rearrange("(m p) n -> p m n", p=P)).then_inc(w2_loaded, 16)
            sp.wait_ge(probs_ready, LOOPS + len(LAST_GROUPS))
            sp.dma_start(out.rearrange("(a b) -> a b", a=1), probs[:]).then_inc(stored, 16)
            sp.wait_ge(stored, 16)

        @block.gpsimd
        def _(pool):
            def gather(slice_, dst, index):
                pool.indirect_dma_start(
                    out=dst, out_offset=None, in_=table,
                    in_offset=bass.IndirectOffsetOnAxis(ap=index, axis=0),
                ).then_inc(gathered[slice_], 16)

            def gather_group(blocks, number):
                for k in ORDER:
                    pool.wait_ge(ids_ready[k], number + 1)
                    pool.sem_inc(may_gather, 1)
                    for b in range(blocks // 2 if k == QUADS else blocks):
                        if k == QUADS:
                            dst, at = pair_rows[:, b, :], b * UNIT + UNIT - 1
                        else:
                            dst, at = quad_rows[:, k, b, :], b // 2 * UNIT + b % 2 * QUADS + k
                        gather(k, dst, group_id[:, at:at + 1])

            with pool.Fori(0, LOOPS) as g:
                gather_group(LOOPED_BLOCKS, g)
            for first, blocks, number in peeled():
                gather_group(blocks, number)

        @block.vector
        def _(dve):
            nc.vector.memset(warm[:], 0.0).then_inc(warm_set, 1)
            nc.vector.memset(weight[:, 0:1], -0.5).then_inc(weight_set, 1)
            nc.vector.memset(weight[:, 1:2], 0.5 / PER_QUAD).then_inc(weight_set, 1)
            dve.wait_ge(slot_loaded, 16)
            raw = slot[:, 0:GATHERS]
            nc.vector.tensor_scalar(wrap[:], raw, 0.0, float(VOCAB), ALU.is_lt, ALU.mult).then_inc(id_step, 1)
            dve.wait_ge(id_step, 1)
            nc.vector.tensor_tensor(wrapped[:], wrap[:], raw, ALU.add).then_inc(id_step, 1)
            dve.wait_ge(id_step, 2)
            nc.vector.tensor_scalar(clamped[:], wrapped[:], 0.0, float(VOCAB - 1),
                                    ALU.max, ALU.min).then_inc(id_step, 1)
            dve.wait_ge(id_step, 3)
            nc.vector.tensor_tensor(row_id[:], clamped[:], slot[:, GATHERS:2 * GATHERS],
                                    ALU.add).then_inc(row_id_ready, 1)
            dve.wait_ge(row_id_ready, 1)

            def slice_ids(ids, k):
                ids = ids.rearrange("p (u c) -> p u c", c=UNIT)
                if k == QUADS:
                    return ids[:, :, UNIT - 1]
                return ids[:, :, 0:UNIT - 1].rearrange("p u (b q) -> p u b q", q=QUADS)[:, :, :, k]

            def place_ids(k, first, blocks):
                ids = blocks // 2 * UNIT
                nc.vector.tensor_copy(slice_ids(group_id[:, 0:ids], k),
                                      slice_ids(row_id[:, bass.ds(first // 2 * UNIT, ids)], k)
                                      ).then_inc(ids_ready[k], 1)

            for k in ORDER:
                place_ids(k, 0, LOOPED_BLOCKS)

            def turn_group(first, blocks, number, following):
                width = blocks * BLOCK
                for k in ORDER:
                    dve.wait_ge(gathered[k], arrived(k, first, blocks))
                    if k == QUADS:
                        both = x_t[0:PAIR, k, 0:width].rearrange("p (n h b) -> p n h b", h=2, b=BLOCK)
                        for h in range(2):
                            nc.vector.transpose(both[:, :, h, :], pair_rows[h * PAIR:(h + 1) * PAIR, 0:blocks // 2, 0:D])
                        nc.vector.tensor_copy(x_t[PAIR:TAIL, k, 0:width],
                                              dense[PAIR:TAIL, bass.ds(first * BLOCK, width)]).then_inc(x_ready, 1)
                        nc.vector.tensor_copy(pair_lin[:, 0:blocks // 2], pair_rows[:, 0:blocks // 2, D]
                                              ).then_inc(taken, 1)
                    else:
                        nc.vector.transpose(x_t[:, k, 0:width].rearrange("p (n b) -> p n b", b=BLOCK),
                                            quad_rows[:, k, 0:blocks, 0:D]).then_inc(x_ready, 1)
                        nc.vector.tensor_copy(lin[:, k, 0:blocks], quad_rows[:, k, 0:blocks, D]
                                              ).then_inc(taken, 1)
                    if following:
                        place_ids(k, *following)

            def sum_group(blocks, number):
                width = blocks * BLOCK
                dve.wait_ge(l0_done, number * M1 + 1)
                dve.wait_ge(taken, (number + 1) * SLICES)
                nc.vector.tensor_reduce(emb_sum[:, 0:width], x_t[:, 0:QUADS, 0:width].rearrange("p q b -> p b q"),
                                        AX.X, ALU.add).then_inc(sum_step, 1)
                nc.vector.tensor_reduce(lin_sum[:, 0:blocks], lin[:, :, 0:blocks].rearrange("p q n -> p n q"),
                                        AX.X, ALU.add).then_inc(sum_step, 1)
                dve.wait_ge(sum_step, number * 3 + 1)
                nc.vector.tensor_tensor(emb_sum[0:PAIR, 0:width], emb_sum[0:PAIR, 0:width],
                                        x_t[0:PAIR, QUADS, 0:width], ALU.add).then_inc(emb_sum_ready, 1)
                dve.wait_ge(sum_step, number * 3 + 2)
                by_half = lin_sum[:, 0:blocks].rearrange("p (n h) -> p n h", h=2)
                for h in range(2):
                    rows_ = slice(h * PAIR, (h + 1) * PAIR)
                    nc.vector.tensor_tensor(by_half[rows_, :, h], by_half[rows_, :, h], pair_lin[rows_, 0:blocks // 2],
                                            ALU.add).then_inc(lin_ready, 1)
                dve.wait_ge(squares_ready, number + 1)
                nc.vector.tensor_reduce(sq_sum[:, 0:width], x_sq[:, 0:QUADS, 0:width].rearrange("p q b -> p b q"),
                                        AX.X, ALU.add).then_inc(sum_step, 1)
                dve.wait_ge(sum_step, number * 3 + 3)
                nc.vector.tensor_tensor(sq_sum[0:PAIR, 0:width], sq_sum[0:PAIR, 0:width],
                                        x_sq[0:PAIR, QUADS, 0:width], ALU.add).then_inc(sq_sum_ready, 1)

            dve.wait_ge(dense_loaded, 16)
            with dve.Fori(0, LOOPS) as g:
                turn_group(g * LOOPED_BLOCKS, LOOPED_BLOCKS, g, ((g + 1) * LOOPED_BLOCKS, LOOPED_BLOCKS))
                sum_group(LOOPED_BLOCKS, g)
            for first, blocks, number in peeled():
                rest = BLOCKS - first - blocks
                turn_group(first, blocks, number, (first + blocks, rest) if rest else None)
                sum_group(blocks, number)

        @block.tensor
        def _(pe):
            def layer(ps_, w, m, k, rhs, start, stop):
                return nc.tensor.matmul(ps_, w[0:rhs.shape[0], k, m * P:m * P + P], rhs,
                                        start=start, stop=stop, skip_group_check=True)

            def multiply_group(blocks, number, load_waits):
                width = blocks * BLOCK
                for i, k in enumerate(ORDER):
                    if load_waits:
                        pe.wait_ge(w0_loaded[k], 16)
                    pe.wait_ge(x_ready, number * SLICES + i + 1)
                    n = TAIL if k == QUADS else P
                    for m in range(M1):
                        mm = layer(ps1[:, m // 2, m % 2, 0:width], w0_sb, m, k, x_t[0:n, k, 0:width],
                                   start=(i == 0 and m % 2 == 0), stop=(i == SLICES - 1))
                        if i == SLICES - 1:
                            mm.then_inc(l0_done, 1)
                early = M1 // 2
                for k in range(early):
                    if load_waits and k * W1_PIECES % M1 == 0:
                        pe.wait_ge(w1_loaded[k * W1_PIECES // M1], 16)
                    pe.wait_ge(h1_ready, number * M1 + k + 1)
                    for m in range(M2):
                        layer(ps2[:, m // 2, m % 2, 0:width], w1_sb, m, k, h1[:, k, 0:width],
                              start=(k == 0 and m % 2 == 0), stop=False)
                for m in range(M2):
                    for k in range(early, M1):
                        if load_waits and m == 0 and k * W1_PIECES % M1 == 0:
                            pe.wait_ge(w1_loaded[k * W1_PIECES // M1], 16)
                        if m == 0:
                            pe.wait_ge(h1_ready, number * M1 + k + 1)
                        mm = layer(ps2[:, m // 2, m % 2, 0:width], w1_sb, m, k, h1[:, k, 0:width],
                                   start=False, stop=(k == M1 - 1))
                    mm.then_inc(l1_done, 1)
                pe.wait_ge(emb_sum_ready, number + 1)
                nc.tensor.matmul(ps_s[:, 0:width], col[:, SEL:SEL + P], emb_sum[:, 0:width],
                                 start=True, stop=True).then_inc(s_done, 1)
                if load_waits:
                    pe.wait_ge(w2_loaded, 16)
                for k in range(M2):
                    pe.wait_ge(h2_ready, number * M2 + k + 1)
                    for m in range(M3):
                        mm = layer(ps3[:, m // 2, m % 2, 0:width], w2_sb, m, k, h2[:, k, 0:width],
                                   start=(k == 0 and m % 2 == 0), stop=(k == M2 - 1))
                        if k == M2 - 1:
                            mm.then_inc(l2_done, 1)
                pe.wait_ge(s_sq_ready, number + 1)
                pe.wait_ge(lin_ready, (number + 1) * 2)
                for b in range(blocks):
                    nc.tensor.matmul(ps_logit[:, b * BLOCK:(b + 1) * BLOCK], lin_sum[:, b:b + 1],
                                     col[:, SEL:SEL + BLOCK], start=(b == 0), stop=False, skip_group_check=True)
                pe.wait_ge(sq_sum_ready, number + 1)
                nc.tensor.matmul(ps_logit[:, 0:width], weight[:, 0:1], sq_sum[:, 0:width],
                                 start=False, stop=False, skip_group_check=True)
                nc.tensor.matmul(ps_logit[:, 0:width], weight[:, 1:2], s_sq[:, 0:width],
                                 start=False, stop=False, skip_group_check=True)
                for k in range(M3):
                    pe.wait_ge(h3_ready, number * M3 + k + 1)
                    mm = nc.tensor.matmul(ps_logit[:, 0:width], col[:, WOUT + k:WOUT + k + 1], h3[:, k, 0:width],
                                          start=False, stop=(k == M3 - 1), skip_group_check=True)
                mm.then_inc(logit_done, 1)

            pe.wait_ge(col_loaded, 16)
            pe.wait_ge(weight_set, 2)
            with pe.Fori(0, LOOPS) as g:
                multiply_group(LOOPED_BLOCKS, g, True)
            for _, blocks, number in peeled():
                multiply_group(blocks, number, False)

        @block.scalar
        def _(act):
            def relu_layer(h, ps_, slices, bias_at, width, number, done, ready):
                for m in range(slices):
                    act.wait_ge(done, number * slices + m // 2 * 2 + 2)
                    nc.scalar.activation(h[:, m, 0:width], ps_[:, m // 2, m % 2, 0:width], ACT.Relu,
                                         bias=col[:, bias_at + m:bias_at + m + 1]).then_inc(ready, 1)

            def activate_group(first, blocks, number):
                width = blocks * BLOCK
                relu_layer(h1, ps1, M1, B0, width, number, l0_done, h1_ready)
                nc.scalar.activation(x_sq[:, 0:QUADS, 0:width], x_t[:, 0:QUADS, 0:width], ACT.Square)
                nc.scalar.activation(x_sq[0:PAIR, QUADS, 0:width], x_t[0:PAIR, QUADS, 0:width],
                                     ACT.Square).then_inc(squares_ready, 1)
                relu_layer(h2, ps2, M2, B1, width, number, l1_done, h2_ready)
                act.wait_ge(s_done, number + 1)
                nc.scalar.activation(s_sq[:, 0:width], ps_s[:, 0:width], ACT.Square).then_inc(s_sq_ready, 1)
                relu_layer(h3, ps3, M3, B2, width, number, l2_done, h3_ready)
                act.wait_ge(logit_done, number + 1)
                nc.scalar.activation(probs[:, bass.ds(first * BLOCK, width)], ps_logit[:, 0:width], ACT.Sigmoid,
                                     bias=col[0:1, BOUT:BOUT + 1]).then_inc(probs_ready, 1)

            act.wait_ge(warm_set, 1)
            nc.scalar.activation(warm[:], warm[:], ACT.Sigmoid)
            act.wait_ge(col_loaded, 16)
            with act.Fori(0, LOOPS) as g:
                activate_group(g * LOOPED_BLOCKS, LOOPED_BLOCKS, g)
            for first, blocks, number in peeled():
                activate_group(first, blocks, number)


def kernel(r_x_dense, r_x_sparse, L0_rec_emb_tables, L0_rec_lin_tables, L0_rec_W0, L0_rec_b0,
           L0_rec_W1, L0_rec_b1, L0_rec_W2, L0_rec_b2, L0_rec_Wout, L0_rec_bout):
    import numpy as np
    import concourse.bacc as bacc
    from concourse.bass_utils import run_bass_kernel_spmd

    emb, lin = np.asarray(L0_rec_emb_tables), np.asarray(L0_rec_lin_tables)
    features, vocab, d = emb.shape
    batch = r_x_sparse.shape[0]
    per_quad = P // BLOCK
    quads = features // per_quad
    blocks = batch // BLOCK

    table = np.concatenate([emb, lin[:, :, None]], axis=2).reshape(features * vocab, d + 1)

    def by_gather(x):
        x = x.reshape(blocks, BLOCK, features)
        quad = x[:, :, :quads * per_quad].reshape(blocks, BLOCK, quads, per_quad)
        quad = quad.transpose(3, 1, 0, 2).reshape(P, blocks // 2, 2 * quads)
        pair = x[:, :, quads * per_quad:].reshape(blocks // 2, 2, BLOCK, features - quads * per_quad)
        pair = pair.transpose(1, 3, 2, 0).reshape(P, blocks // 2, 1)
        return np.concatenate([quad, pair], axis=2).reshape(P, -1)

    first_row = np.broadcast_to(np.arange(0, features * vocab, vocab, dtype=np.int32), (batch, features))
    slots = np.concatenate([by_gather(np.asarray(r_x_sparse)), by_gather(first_row)], axis=1)

    def in_columns(v):
        return np.asarray(v).reshape(-1, P).T

    bout = np.broadcast_to(np.asarray(L0_rec_bout).reshape(1, 1), (P, 1))
    sel = np.tile(np.eye(BLOCK, dtype=np.float32), (per_quad, per_quad))
    columns = np.concatenate([in_columns(L0_rec_b0), in_columns(L0_rec_b1), in_columns(L0_rec_b2),
                              in_columns(L0_rec_Wout), bout, sel], axis=1)
    arrays = {
        "table": table, "slots": slots, "w0": np.asarray(L0_rec_W0), "w1": np.asarray(L0_rec_W1),
        "w2": np.asarray(L0_rec_W2), "dense_t": np.asarray(r_x_dense).T, "columns": columns,
    }
    arrays = {k: np.ascontiguousarray(a) for k, a in arrays.items()}

    nc = bacc.Bacc("TRN2", target_bir_lowering=False, num_devices=1)
    args = [nc.dram_tensor(k, a.shape, mybir.dt.from_np(a.dtype), kind="ExternalInput").ap()
            for k, a in arrays.items()]
    out = nc.dram_tensor("out", (batch,), F32, kind="ExternalOutput").ap()
    deepfm(nc, *args, out)
    r = run_bass_kernel_spmd(nc, [arrays], core_ids=[0])
    return r.results[0]["out"]
```

```python
from contextlib import ExitStack

import concourse.bass as bass
from concourse import mybir

ALU = mybir.AluOpType
ACT = mybir.ActivationFunctionType
AX = mybir.AxisListType
F32 = mybir.dt.float32
I32 = mybir.dt.int32

P = 128
BLOCK = 32
BANK = 512
GROUP = 4


def deepfm(nc, table, slots, w0, w1, w2, dense_t, columns, out):
    rows, ROW = table.shape
    D = ROW - 1
    BATCH = out.shape[0]
    DENSE = dense_t.shape[0]
    IN, H1 = w0.shape
    H2, H3 = w2.shape
    FEATURES = (IN - DENSE) // D
    VOCAB = rows // FEATURES
    PER_QUAD = P // BLOCK
    QUADS = FEATURES // PER_QUAD
    TAIL = IN - QUADS * P
    PAIR = TAIL - DENSE
    assert D == BLOCK and PAIR == P // 2
    BLOCKS = BATCH // BLOCK
    UNIT = 2 * QUADS + 1
    GATHERS = BLOCKS // 2 * UNIT
    GROUP_IDS = GROUP // 2 * UNIT
    M1, M2, M3 = H1 // P, H2 // P, H3 // P
    SLICES = QUADS + 1
    ORDER = [QUADS] + list(range(QUADS))
    GROUPS = BLOCKS // GROUP
    WIDTH = GROUP * BLOCK
    W1_PIECES = 4
    B0, B1, B2 = 0, M1, M1 + M2
    WOUT = B2 + M3
    BOUT = WOUT + M3
    SEL = BOUT + 1
    COLUMNS = columns.shape[1]

    def arrived(slice_, groups):
        return groups * (GROUP // 2 if slice_ == QUADS else GROUP) * 16

    with ExitStack() as ctx:
        def sb(name, shape, dt=F32):
            return ctx.enter_context(nc.sbuf_tensor(name, shape, dt))

        def ps(name, shape):
            return ctx.enter_context(nc.psum_tensor(name, shape, F32))

        def sem(name):
            return ctx.enter_context(nc.semaphore(name))

        slot = sb("slot", [P, 2 * GATHERS], I32)
        wrap = sb("wrap", [P, GATHERS])
        wrapped = sb("wrapped", [P, GATHERS])
        clamped = sb("clamped", [P, GATHERS])
        row_id = sb("row_id", [P, GATHERS + GROUP_IDS], I32)
        group_id = sb("group_id", [P, GROUP_IDS], I32)
        quad_rows = sb("quad_rows", [P, QUADS, GROUP, ROW])
        pair_rows = sb("pair_rows", [P, GROUP // 2, ROW])
        dense = sb("dense", [P, BATCH])
        x_t = sb("x_t", [P, SLICES, WIDTH])
        w0_sb = sb("w0_sb", [P, SLICES, H1])
        w1_sb = sb("w1_sb", [P, M1, H2])
        w2_sb = sb("w2_sb", [P, M2, H3])
        col = sb("col", [P, COLUMNS])
        weight = sb("weight", [P, 2])
        warm = sb("warm", [1, 1])
        h1 = sb("h1", [P, M1, WIDTH])
        h2 = sb("h2", [P, M2, WIDTH])
        h3 = sb("h3", [P, M3, WIDTH])
        lin = sb("lin", [P, QUADS, GROUP])
        pair_lin = sb("pair_lin", [P, GROUP // 2])
        lin_sum = sb("lin_sum", [P, GROUP])
        x_sq = sb("x_sq", [P, SLICES, WIDTH])
        emb_sum = sb("emb_sum", [P, WIDTH])
        sq_sum = sb("sq_sum", [P, WIDTH])
        s_sq = sb("s_sq", [P, WIDTH])
        probs = sb("probs", [1, BATCH])

        ps1 = ps("ps1", [P, M1 // 2, 2, BANK // 2])
        ps2 = ps("ps2", [P, M2 // 2, 2, BANK // 2])
        ps3 = ps("ps3", [P, M3 // 2, 2, BANK // 2])
        ps_row = ps("ps_row", [P, 2, BANK // 2])
        ps_s, ps_logit = ps_row[:, 0, :], ps_row[0:1, 1, :]

        slot_loaded = sem("slot_loaded")
        col_loaded = sem("col_loaded")
        dense_loaded = sem("dense_loaded")
        w0_loaded = [sem(f"w0_loaded{k}") for k in range(SLICES)]
        w1_loaded = [sem(f"w1_loaded{k}") for k in range(W1_PIECES)]
        w2_loaded = sem("w2_loaded")
        warm_set = sem("warm_set")
        weight_set = sem("weight_set")
        id_step = sem("id_step")
        row_id_ready = sem("row_id_ready")
        ids_ready = [sem(f"ids_ready{k}") for k in range(SLICES)]
        may_gather = sem("may_gather")
        gathered = [sem(f"gathered{k}") for k in range(SLICES)]
        x_ready = sem("x_ready")
        l0_done = sem("l0_done")
        h1_ready = sem("h1_ready")
        l1_done = sem("l1_done")
        h2_ready = sem("h2_ready")
        l2_done = sem("l2_done")
        h3_ready = sem("h3_ready")
        taken = sem("taken")
        sum_step = sem("sum_step")
        squares_ready = sem("squares_ready")
        emb_sum_ready = sem("emb_sum_ready")
        lin_ready = sem("lin_ready")
        sq_sum_ready = sem("sq_sum_ready")
        s_done = sem("s_done")
        s_sq_ready = sem("s_sq_ready")
        logit_done = sem("logit_done")
        probs_ready = sem("probs_ready")
        stored = sem("stored")

        block = ctx.enter_context(nc.Block())

        @block.sync
        def _(sp):
            sp.dma_start(slot[:], slots).then_inc(slot_loaded, 16)
            sp.dma_start(dense[PAIR:TAIL, :], dense_t).then_inc(dense_loaded, 16)
            sp.dma_start(w0_sb[0:TAIL, QUADS, :], w0[QUADS * P:IN, :]).then_inc(w0_loaded[QUADS], 16)
            sp.dma_start(col[:], columns).then_inc(col_loaded, 16)
            for i, k in enumerate(ORDER[1:]):
                if i:
                    before = ORDER[i - 1]
                    sp.wait_ge(gathered[before], arrived(before, 1))
                sp.dma_start(w0_sb[:, k, :], w0[k * P:k * P + P, :]).then_inc(w0_loaded[k], 16)
            w1_rows = w1.rearrange("(m p) n -> p m n", p=P)
            for piece in range(W1_PIECES):
                if piece < 2:
                    before = ORDER[SLICES - 2 + piece]
                    sp.wait_ge(gathered[before], arrived(before, 1))
                else:
                    before = ORDER[piece - 2]
                    sp.wait_ge(gathered[before], arrived(before, 2))
                some = slice(piece * M1 // W1_PIECES, (piece + 1) * M1 // W1_PIECES)
                sp.dma_start(w1_sb[:, some, :], w1_rows[:, some, :]).then_inc(w1_loaded[piece], 16)
            sp.dma_start(w2_sb[:], w2.rearrange("(m p) n -> p m n", p=P)).then_inc(w2_loaded, 16)
            sp.wait_ge(probs_ready, GROUPS)
            sp.dma_start(out.rearrange("(a b) -> a b", a=1), probs[:]).then_inc(stored, 16)
            sp.wait_ge(stored, 16)

        @block.gpsimd
        def _(pool):
            def gather(slice_, dst, index):
                pool.indirect_dma_start(
                    out=dst, out_offset=None, in_=table,
                    in_offset=bass.IndirectOffsetOnAxis(ap=index, axis=0),
                ).then_inc(gathered[slice_], 16)

            def gather_group(number):
                for k in ORDER:
                    pool.wait_ge(ids_ready[k], number + 1)
                    pool.sem_inc(may_gather, 1)
                    for b in range(GROUP // 2 if k == QUADS else GROUP):
                        if k == QUADS:
                            dst, at = pair_rows[:, b, :], b * UNIT + UNIT - 1
                        else:
                            dst, at = quad_rows[:, k, b, :], b // 2 * UNIT + b % 2 * QUADS + k
                        gather(k, dst, group_id[:, at:at + 1])

            with pool.Fori(0, GROUPS) as g:
                gather_group(g)

        @block.vector
        def _(dve):
            nc.vector.memset(warm[:], 0.0).then_inc(warm_set, 1)
            nc.vector.memset(weight[:, 0:1], -0.5).then_inc(weight_set, 1)
            nc.vector.memset(weight[:, 1:2], 0.5 / PER_QUAD).then_inc(weight_set, 1)
            nc.vector.memset(row_id[:, GATHERS:], 0).then_inc(row_id_ready, 1)
            dve.wait_ge(slot_loaded, 16)
            raw = slot[:, 0:GATHERS]
            nc.vector.tensor_scalar(wrap[:], raw, 0.0, float(VOCAB), ALU.is_lt, ALU.mult).then_inc(id_step, 1)
            dve.wait_ge(id_step, 1)
            nc.vector.tensor_tensor(wrapped[:], wrap[:], raw, ALU.add).then_inc(id_step, 1)
            dve.wait_ge(id_step, 2)
            nc.vector.tensor_scalar(clamped[:], wrapped[:], 0.0, float(VOCAB - 1),
                                    ALU.max, ALU.min).then_inc(id_step, 1)
            dve.wait_ge(id_step, 3)
            nc.vector.tensor_tensor(row_id[:, 0:GATHERS], clamped[:], slot[:, GATHERS:2 * GATHERS],
                                    ALU.add).then_inc(row_id_ready, 1)
            dve.wait_ge(row_id_ready, 2)

            def slice_ids(ids, k):
                ids = ids.rearrange("p (u c) -> p u c", c=UNIT)
                if k == QUADS:
                    return ids[:, :, UNIT - 1]
                return ids[:, :, 0:UNIT - 1].rearrange("p u (b q) -> p u b q", q=QUADS)[:, :, :, k]

            def place_ids(k, number):
                nc.vector.tensor_copy(slice_ids(group_id, k),
                                      slice_ids(row_id[:, bass.ds(number * GROUP_IDS, GROUP_IDS)], k)
                                      ).then_inc(ids_ready[k], 1)

            for k in ORDER:
                place_ids(k, 0)

            def turn_group(number):
                for k in ORDER:
                    dve.wait_ge(gathered[k], arrived(k, number + 1))
                    if k == QUADS:
                        both = x_t[0:PAIR, k, 0:WIDTH].rearrange("p (n h b) -> p n h b", h=2, b=BLOCK)
                        for h in range(2):
                            nc.vector.transpose(both[:, :, h, :], pair_rows[h * PAIR:(h + 1) * PAIR, 0:GROUP // 2, 0:D])
                        nc.vector.tensor_copy(x_t[PAIR:TAIL, k, 0:WIDTH],
                                              dense[PAIR:TAIL, bass.ds(number * WIDTH, WIDTH)]).then_inc(x_ready, 1)
                        nc.vector.tensor_copy(pair_lin[:, 0:GROUP // 2], pair_rows[:, 0:GROUP // 2, D]
                                              ).then_inc(taken, 1)
                    else:
                        nc.vector.transpose(x_t[:, k, :].rearrange("p (n b) -> p n b", b=BLOCK),
                                            quad_rows[:, k, 0:GROUP, 0:D]).then_inc(x_ready, 1)
                        nc.vector.tensor_copy(lin[:, k, 0:GROUP], quad_rows[:, k, 0:GROUP, D]
                                              ).then_inc(taken, 1)
                    place_ids(k, number + 1)

            def sum_group(number):
                dve.wait_ge(l0_done, number * M1 + 1)
                dve.wait_ge(taken, (number + 1) * SLICES)
                nc.vector.tensor_reduce(emb_sum[:, 0:WIDTH], x_t[:, 0:QUADS, 0:WIDTH].rearrange("p q b -> p b q"),
                                        AX.X, ALU.add).then_inc(sum_step, 1)
                nc.vector.tensor_reduce(lin_sum[:, 0:GROUP], lin[:, :, 0:GROUP].rearrange("p q n -> p n q"),
                                        AX.X, ALU.add).then_inc(sum_step, 1)
                dve.wait_ge(sum_step, number * 3 + 1)
                nc.vector.tensor_tensor(emb_sum[0:PAIR, 0:WIDTH], emb_sum[0:PAIR, 0:WIDTH],
                                        x_t[0:PAIR, QUADS, 0:WIDTH], ALU.add).then_inc(emb_sum_ready, 1)
                dve.wait_ge(sum_step, number * 3 + 2)
                by_half = lin_sum[:, 0:GROUP].rearrange("p (n h) -> p n h", h=2)
                for h in range(2):
                    rows_ = slice(h * PAIR, (h + 1) * PAIR)
                    nc.vector.tensor_tensor(by_half[rows_, :, h], by_half[rows_, :, h], pair_lin[rows_, 0:GROUP // 2],
                                            ALU.add).then_inc(lin_ready, 1)
                dve.wait_ge(squares_ready, number + 1)
                nc.vector.tensor_reduce(sq_sum[:, 0:WIDTH], x_sq[:, 0:QUADS, 0:WIDTH].rearrange("p q b -> p b q"),
                                        AX.X, ALU.add).then_inc(sum_step, 1)
                dve.wait_ge(sum_step, number * 3 + 3)
                nc.vector.tensor_tensor(sq_sum[0:PAIR, 0:WIDTH], sq_sum[0:PAIR, 0:WIDTH],
                                        x_sq[0:PAIR, QUADS, 0:WIDTH], ALU.add).then_inc(sq_sum_ready, 1)

            dve.wait_ge(dense_loaded, 16)
            with dve.Fori(0, GROUPS) as g:
                turn_group(g)
                sum_group(g)

        @block.tensor
        def _(pe):
            def layer(ps_, w, m, k, rhs, start, stop):
                return nc.tensor.matmul(ps_, w[0:rhs.shape[0], k, m * P:m * P + P], rhs,
                                        start=start, stop=stop, skip_group_check=True)

            def multiply_group(number):
                for i, k in enumerate(ORDER):
                    pe.wait_ge(w0_loaded[k], 16)
                    pe.wait_ge(x_ready, number * SLICES + i + 1)
                    n = TAIL if k == QUADS else P
                    for m in range(M1):
                        mm = layer(ps1[:, m // 2, m % 2, 0:WIDTH], w0_sb, m, k, x_t[0:n, k, 0:WIDTH],
                                   start=(i == 0 and m % 2 == 0), stop=(i == SLICES - 1))
                        if i == SLICES - 1:
                            mm.then_inc(l0_done, 1)
                early = M1 // 2
                for k in range(early):
                    if k * W1_PIECES % M1 == 0:
                        pe.wait_ge(w1_loaded[k * W1_PIECES // M1], 16)
                    pe.wait_ge(h1_ready, number * M1 + k + 1)
                    for m in range(M2):
                        layer(ps2[:, m // 2, m % 2, 0:WIDTH], w1_sb, m, k, h1[:, k, :],
                              start=(k == 0 and m % 2 == 0), stop=False)
                for m in range(M2):
                    for k in range(early, M1):
                        if m == 0 and k * W1_PIECES % M1 == 0:
                            pe.wait_ge(w1_loaded[k * W1_PIECES // M1], 16)
                        if m == 0:
                            pe.wait_ge(h1_ready, number * M1 + k + 1)
                        mm = layer(ps2[:, m // 2, m % 2, 0:WIDTH], w1_sb, m, k, h1[:, k, :],
                                   start=False, stop=(k == M1 - 1))
                    mm.then_inc(l1_done, 1)
                pe.wait_ge(emb_sum_ready, number + 1)
                nc.tensor.matmul(ps_s[:, 0:WIDTH], col[:, SEL:SEL + P], emb_sum[:, 0:WIDTH],
                                 start=True, stop=True).then_inc(s_done, 1)
                pe.wait_ge(w2_loaded, 16)
                for k in range(M2):
                    pe.wait_ge(h2_ready, number * M2 + k + 1)
                    for m in range(M3):
                        mm = layer(ps3[:, m // 2, m % 2, 0:WIDTH], w2_sb, m, k, h2[:, k, :],
                                   start=(k == 0 and m % 2 == 0), stop=(k == M2 - 1))
                        if k == M2 - 1:
                            mm.then_inc(l2_done, 1)
                pe.wait_ge(s_sq_ready, number + 1)
                pe.wait_ge(lin_ready, (number + 1) * 2)
                for b in range(GROUP):
                    nc.tensor.matmul(ps_logit[:, b * BLOCK:(b + 1) * BLOCK], lin_sum[:, b:b + 1],
                                     col[:, SEL:SEL + BLOCK], start=(b == 0), stop=False, skip_group_check=True)
                pe.wait_ge(sq_sum_ready, number + 1)
                nc.tensor.matmul(ps_logit[:, 0:WIDTH], weight[:, 0:1], sq_sum[:, 0:WIDTH],
                                 start=False, stop=False, skip_group_check=True)
                nc.tensor.matmul(ps_logit[:, 0:WIDTH], weight[:, 1:2], s_sq[:, 0:WIDTH],
                                 start=False, stop=False, skip_group_check=True)
                for k in range(M3):
                    pe.wait_ge(h3_ready, number * M3 + k + 1)
                    mm = nc.tensor.matmul(ps_logit[:, 0:WIDTH], col[:, WOUT + k:WOUT + k + 1], h3[:, k, :],
                                          start=False, stop=(k == M3 - 1), skip_group_check=True)
                mm.then_inc(logit_done, 1)

            pe.wait_ge(col_loaded, 16)
            pe.wait_ge(weight_set, 2)
            with pe.Fori(0, GROUPS) as g:
                multiply_group(g)

        @block.scalar
        def _(act):
            def relu_layer(h, ps_, slices, bias_at, number, done, ready):
                for m in range(slices):
                    act.wait_ge(done, number * slices + m // 2 * 2 + 2)
                    nc.scalar.activation(h[:, m, :], ps_[:, m // 2, m % 2, 0:WIDTH], ACT.Relu,
                                         bias=col[:, bias_at + m:bias_at + m + 1]).then_inc(ready, 1)

            def activate_group(number):
                relu_layer(h1, ps1, M1, B0, number, l0_done, h1_ready)
                nc.scalar.activation(x_sq[:, 0:QUADS, 0:WIDTH], x_t[:, 0:QUADS, 0:WIDTH], ACT.Square)
                nc.scalar.activation(x_sq[0:PAIR, QUADS, 0:WIDTH], x_t[0:PAIR, QUADS, 0:WIDTH],
                                     ACT.Square).then_inc(squares_ready, 1)
                relu_layer(h2, ps2, M2, B1, number, l1_done, h2_ready)
                act.wait_ge(s_done, number + 1)
                nc.scalar.activation(s_sq[:, 0:WIDTH], ps_s[:, 0:WIDTH], ACT.Square).then_inc(s_sq_ready, 1)
                relu_layer(h3, ps3, M3, B2, number, l2_done, h3_ready)
                act.wait_ge(logit_done, number + 1)
                nc.scalar.activation(probs[:, bass.ds(number * WIDTH, WIDTH)], ps_logit[:, 0:WIDTH], ACT.Sigmoid,
                                     bias=col[0:1, BOUT:BOUT + 1]).then_inc(probs_ready, 1)

            act.wait_ge(warm_set, 1)
            nc.scalar.activation(warm[:], warm[:], ACT.Sigmoid)
            act.wait_ge(col_loaded, 16)
            with act.Fori(0, GROUPS) as g:
                activate_group(g)


def kernel(r_x_dense, r_x_sparse, L0_rec_emb_tables, L0_rec_lin_tables, L0_rec_W0, L0_rec_b0,
           L0_rec_W1, L0_rec_b1, L0_rec_W2, L0_rec_b2, L0_rec_Wout, L0_rec_bout):
    import numpy as np
    import concourse.bacc as bacc
    from concourse.bass_utils import run_bass_kernel_spmd

    emb, lin = np.asarray(L0_rec_emb_tables), np.asarray(L0_rec_lin_tables)
    features, vocab, d = emb.shape
    batch = r_x_sparse.shape[0]
    per_quad = P // BLOCK
    quads = features // per_quad
    blocks = batch // BLOCK

    table = np.concatenate([emb, lin[:, :, None]], axis=2).reshape(features * vocab, d + 1)

    def by_gather(x):
        x = x.reshape(blocks, BLOCK, features)
        quad = x[:, :, :quads * per_quad].reshape(blocks, BLOCK, quads, per_quad)
        quad = quad.transpose(3, 1, 0, 2).reshape(P, blocks // 2, 2 * quads)
        pair = x[:, :, quads * per_quad:].reshape(blocks // 2, 2, BLOCK, features - quads * per_quad)
        pair = pair.transpose(1, 3, 2, 0).reshape(P, blocks // 2, 1)
        return np.concatenate([quad, pair], axis=2).reshape(P, -1)

    first_row = np.broadcast_to(np.arange(0, features * vocab, vocab, dtype=np.int32), (batch, features))
    slots = np.concatenate([by_gather(np.asarray(r_x_sparse)), by_gather(first_row)], axis=1)

    def in_columns(v):
        return np.asarray(v).reshape(-1, P).T

    bout = np.broadcast_to(np.asarray(L0_rec_bout).reshape(1, 1), (P, 1))
    sel = np.tile(np.eye(BLOCK, dtype=np.float32), (per_quad, per_quad))
    columns = np.concatenate([in_columns(L0_rec_b0), in_columns(L0_rec_b1), in_columns(L0_rec_b2),
                              in_columns(L0_rec_Wout), bout, sel], axis=1)
    arrays = {
        "table": table, "slots": slots, "w0": np.asarray(L0_rec_W0), "w1": np.asarray(L0_rec_W1),
        "w2": np.asarray(L0_rec_W2), "dense_t": np.asarray(r_x_dense).T, "columns": columns,
    }
    arrays = {k: np.ascontiguousarray(a) for k, a in arrays.items()}

    nc = bacc.Bacc("TRN2", target_bir_lowering=False, num_devices=1)
    args = [nc.dram_tensor(k, a.shape, mybir.dt.from_np(a.dtype), kind="ExternalInput").ap()
            for k, a in arrays.items()]
    out = nc.dram_tensor("out", (batch,), F32, kind="ExternalOutput").ap()
    deepfm(nc, *args, out)
    r = run_bass_kernel_spmd(nc, [arrays], core_ids=[0])
    return r.results[0]["out"]
```

```python
from contextlib import ExitStack

import concourse.bass as bass
from concourse import mybir

ALU = mybir.AluOpType
ACT = mybir.ActivationFunctionType
AX = mybir.AxisListType
F32 = mybir.dt.float32
I32 = mybir.dt.int32

P = 128
BLOCK = 32
BANK = 512
GROUP = 4


def deepfm(nc, table, slots, w0, w1, w2, dense_t, columns, out):
    rows, ROW = table.shape
    D = ROW - 1
    BATCH = out.shape[0]
    DENSE = dense_t.shape[0]
    IN, H1 = w0.shape
    H2, H3 = w2.shape
    FEATURES = (IN - DENSE) // D
    VOCAB = rows // FEATURES
    PER_QUAD = P // BLOCK
    QUADS = FEATURES // PER_QUAD
    TAIL = IN - QUADS * P
    PAIR = TAIL - DENSE
    assert D == BLOCK and PAIR == P // 2 and H3 == 2 * P
    BLOCKS = BATCH // BLOCK
    UNIT = 2 * QUADS + 1
    GATHERS = BLOCKS // 2 * UNIT
    GROUP_IDS = GROUP // 2 * UNIT
    M1, M2, M3 = H1 // P, H2 // P, H3 // P
    SLICES = QUADS + 1
    ORDER = [QUADS] + list(range(QUADS))
    GROUPS = BLOCKS // GROUP
    WIDTH = GROUP * BLOCK
    W1_PIECES = 4
    B0, B1, B2 = 0, M1, M1 + M2
    WOUT = B2 + M3
    BOUT = WOUT + M3
    SEL = BOUT + 1
    COLUMNS = columns.shape[1]

    def arrived(slice_, groups):
        return groups * (GROUP // 2 if slice_ == QUADS else GROUP) * 16

    with ExitStack() as ctx:
        def sb(name, shape, dt=F32):
            return ctx.enter_context(nc.sbuf_tensor(name, shape, dt))

        def ps(name, shape):
            return ctx.enter_context(nc.psum_tensor(name, shape, F32))

        def sem(name):
            return ctx.enter_context(nc.semaphore(name))

        slot = sb("slot", [P, 2, GATHERS], I32)
        wrap = sb("wrap", [P, GATHERS])
        wrapped = sb("wrapped", [P, GATHERS])
        low = sb("low", [P, GATHERS])
        row_id = sb("row_id", [P, GATHERS + GROUP_IDS], I32)
        group_id = sb("group_id", [P, GROUP_IDS], I32)
        quad_rows = sb("quad_rows", [P, QUADS, GROUP, ROW])
        pair_rows = sb("pair_rows", [P, GROUP // 2, ROW])
        dense = sb("dense", [P, BATCH])
        x_t = sb("x_t", [P, SLICES, WIDTH])
        w0_sb = sb("w0_sb", [P, SLICES, H1])
        w1_sb = sb("w1_sb", [P, M1, H2])
        w2_sb = sb("w2_sb", [P, M2, H3])
        col = sb("col", [P, COLUMNS])
        weight = sb("weight", [P, 2])
        warm = sb("warm", [1, 1])
        h1 = sb("h1", [P, M1, WIDTH])
        h2 = sb("h2", [P, M2, WIDTH])
        h3 = sb("h3", [P, M3, WIDTH])
        lin = sb("lin", [P, QUADS, GROUP])
        pair_lin = sb("pair_lin", [P, GROUP // 2])
        lin_sum = sb("lin_sum", [P, GROUP])
        x_sq = sb("x_sq", [P, SLICES, WIDTH])
        emb_sum = sb("emb_sum", [P, WIDTH])
        sq_sum = sb("sq_sum", [P, WIDTH])
        lin_wide = sb("lin_wide", [P, WIDTH])
        row_part = sb("row_part", [P, WIDTH])
        s_sq = sb("s_sq", [P, WIDTH])
        probs = sb("probs", [1, BATCH])

        ps1 = ps("ps1", [P, M1 // 2, 2, BANK // 2])
        ps2 = ps("ps2", [P, M2 // 2, 2, BANK // 2])
        ps3 = ps("ps3", [P, BANK])
        ps_row = ps("ps_row", [P, BANK])
        l0_out = [ps1[:, m // 2, m % 2, 0:WIDTH] for m in range(M1)]
        l1_out = [ps2[:, m // 2, m % 2, 0:WIDTH] for m in range(M2)]
        l2_out = [ps3[:, 0:WIDTH], ps1[:, 1, 1, WIDTH:2 * WIDTH]]
        emb_sum_out = ps1[:, 0, 1, WIDTH:2 * WIDTH]
        logit_row = ps_row[0:1, 0:WIDTH]

        slot_loaded = [sem(f"slot_loaded{n}") for n in range(2)]
        col_loaded = sem("col_loaded")
        dense_loaded = sem("dense_loaded")
        w0_loaded = [sem(f"w0_loaded{k}") for k in range(SLICES)]
        w1_loaded = [sem(f"w1_loaded{k}") for k in range(W1_PIECES)]
        w2_loaded = sem("w2_loaded")
        warm_set = sem("warm_set")
        weight_set = sem("weight_set")
        id_step = sem("id_step")
        first_ids_ready = sem("first_ids_ready")
        row_id_ready = sem("row_id_ready")
        ids_ready = [sem(f"ids_ready{k}") for k in range(SLICES)]
        may_gather = sem("may_gather")
        gathered = [sem(f"gathered{k}") for k in range(SLICES)]
        x_ready = sem("x_ready")
        l0_done = sem("l0_done")
        h1_ready = sem("h1_ready")
        l1_done = sem("l1_done")
        h2_ready = sem("h2_ready")
        l2_done = sem("l2_done")
        h3_ready = sem("h3_ready")
        taken = sem("taken")
        sum_step = sem("sum_step")
        squares_ready = sem("squares_ready")
        emb_sum_ready = sem("emb_sum_ready")
        lin_ready = sem("lin_ready")
        lin_wide_ready = sem("lin_wide_ready")
        row_part_ready = sem("row_part_ready")
        sq_sum_ready = sem("sq_sum_ready")
        s_done = sem("s_done")
        s_sq_ready = sem("s_sq_ready")
        logit_done = sem("logit_done")
        probs_ready = sem("probs_ready")
        stored = sem("stored")

        block = ctx.enter_context(nc.Block())

        @block.sync
        def _(sp):
            for n, some in enumerate((slice(0, GROUP_IDS), slice(GROUP_IDS, GATHERS))):
                sp.dma_start(slot[:, :, some], slots[:, :, some]).then_inc(slot_loaded[n], 16)
            sp.dma_start(dense[PAIR:TAIL, :], dense_t).then_inc(dense_loaded, 16)
            sp.dma_start(w0_sb[0:TAIL, QUADS, :], w0[QUADS * P:IN, :]).then_inc(w0_loaded[QUADS], 16)
            sp.dma_start(col[:], columns).then_inc(col_loaded, 16)
            for i, k in enumerate(ORDER[1:]):
                if i:
                    before = ORDER[i - 1]
                    sp.wait_ge(gathered[before], arrived(before, 1))
                sp.dma_start(w0_sb[:, k, :], w0[k * P:k * P + P, :]).then_inc(w0_loaded[k], 16)
            w1_rows = w1.rearrange("(m p) n -> p m n", p=P)
            for piece in range(W1_PIECES):
                if piece < 2:
                    before = ORDER[SLICES - 2 + piece]
                    sp.wait_ge(gathered[before], arrived(before, 1))
                else:
                    before = ORDER[piece - 2]
                    sp.wait_ge(gathered[before], arrived(before, 2))
                some = slice(piece * M1 // W1_PIECES, (piece + 1) * M1 // W1_PIECES)
                sp.dma_start(w1_sb[:, some, :], w1_rows[:, some, :]).then_inc(w1_loaded[piece], 16)
            sp.dma_start(w2_sb[:], w2.rearrange("(m p) n -> p m n", p=P)).then_inc(w2_loaded, 16)
            sp.wait_ge(probs_ready, GROUPS)
            sp.dma_start(out.rearrange("(a b) -> a b", a=1), probs[:]).then_inc(stored, 16)
            sp.wait_ge(stored, 16)

        @block.gpsimd
        def _(pool):
            def gather(slice_, dst, index):
                pool.indirect_dma_start(
                    out=dst, out_offset=None, in_=table,
                    in_offset=bass.IndirectOffsetOnAxis(ap=index, axis=0),
                ).then_inc(gathered[slice_], 16)

            def gather_group(number):
                for k in ORDER:
                    pool.wait_ge(ids_ready[k], number + 1)
                    pool.sem_inc(may_gather, 1)
                    for b in range(GROUP // 2 if k == QUADS else GROUP):
                        if k == QUADS:
                            dst, at = pair_rows[:, b, :], b * UNIT + UNIT - 1
                        else:
                            dst, at = quad_rows[:, k, b, :], b // 2 * UNIT + b % 2 * QUADS + k
                        gather(k, dst, group_id[:, at:at + 1])

            for k in ORDER:
                pool.sem_inc(ids_ready[k], 1)
            pool.wait_ge(first_ids_ready, 1)
            with pool.Fori(0, GROUPS) as g:
                gather_group(g)

        @block.vector
        def _(dve):
            nc.vector.memset(warm[:], 0.0).then_inc(warm_set, 1)
            nc.vector.memset(weight[:, 0:1], 1.0).then_inc(weight_set, 1)
            nc.vector.memset(weight[:, 1:2], 0.5 / PER_QUAD).then_inc(weight_set, 1)
            nc.vector.memset(row_id[:, GATHERS:], 0).then_inc(row_id_ready, 1)

            def row_ids(ids, at, count, step):
                raw, row0 = slot[:, 0, at:at + count], slot[:, 1, at:at + count]
                wrap_, low_, sum_ = (x[:, at:at + count] for x in (wrap, low, wrapped))
                nc.vector.tensor_scalar(wrap_, raw, 0.0, float(VOCAB), ALU.is_lt, ALU.mult).then_inc(id_step, 1)
                nc.vector.scalar_tensor_tensor(low_, raw, float(VOCAB - 1), row0, ALU.min, ALU.add
                                               ).then_inc(id_step, 1)
                dve.wait_ge(id_step, step + 2)
                nc.vector.tensor_tensor(sum_, wrap_, low_, ALU.add).then_inc(id_step, 1)
                dve.wait_ge(id_step, step + 3)
                return nc.vector.tensor_tensor(ids, sum_, row0, ALU.max)

            dve.wait_ge(slot_loaded[0], 16)
            row_ids(group_id[:], 0, GROUP_IDS, 0).then_inc(first_ids_ready, 1)
            dve.wait_ge(slot_loaded[1], 16)
            row_ids(row_id[:, GROUP_IDS:GATHERS], GROUP_IDS, GATHERS - GROUP_IDS, 3).then_inc(row_id_ready, 1)
            dve.wait_ge(row_id_ready, 2)

            def slice_ids(ids, k):
                ids = ids.rearrange("p (u c) -> p u c", c=UNIT)
                if k == QUADS:
                    return ids[:, :, UNIT - 1]
                return ids[:, :, 0:UNIT - 1].rearrange("p u (b q) -> p u b q", q=QUADS)[:, :, :, k]

            def place_ids(k, number):
                nc.vector.tensor_copy(slice_ids(group_id, k),
                                      slice_ids(row_id[:, bass.ds(number * GROUP_IDS, GROUP_IDS)], k)
                                      ).then_inc(ids_ready[k], 1)

            def turn_group(number):
                for k in ORDER:
                    dve.wait_ge(gathered[k], arrived(k, number + 1))
                    if k == QUADS:
                        both = x_t[0:PAIR, k].rearrange("p (n h b) -> p n h b", h=2, b=BLOCK)
                        for h in range(2):
                            nc.vector.transpose(both[:, :, h, :], pair_rows[h * PAIR:(h + 1) * PAIR, :, 0:D])
                        nc.vector.tensor_copy(x_t[PAIR:TAIL, k],
                                              dense[PAIR:TAIL, bass.ds(number * WIDTH, WIDTH)]).then_inc(x_ready, 1)
                        nc.vector.tensor_copy(pair_lin[:], pair_rows[:, :, D]
                                              ).then_inc(taken, 1)
                    else:
                        nc.vector.transpose(x_t[:, k, :].rearrange("p (n b) -> p n b", b=BLOCK),
                                            quad_rows[:, k, :, 0:D]).then_inc(x_ready, 1)
                        nc.vector.tensor_copy(lin[:, k, :], quad_rows[:, k, :, D]
                                              ).then_inc(taken, 1)
                    place_ids(k, number + 1)

            def sum_group(number):
                dve.wait_ge(l0_done, number * M1 + 1)
                dve.wait_ge(taken, (number + 1) * SLICES)
                nc.vector.tensor_reduce(emb_sum[:], x_t[:, 0:QUADS].rearrange("p q b -> p b q"),
                                        AX.X, ALU.add).then_inc(sum_step, 1)
                nc.vector.tensor_reduce(lin_sum[:], lin[:].rearrange("p q n -> p n q"),
                                        AX.X, ALU.add).then_inc(sum_step, 1)
                dve.wait_ge(sum_step, number * 3 + 1)
                nc.vector.tensor_tensor(emb_sum[0:PAIR], emb_sum[0:PAIR],
                                        x_t[0:PAIR, QUADS], ALU.add).then_inc(emb_sum_ready, 1)
                dve.wait_ge(sum_step, number * 3 + 2)
                by_half = lin_sum[:].rearrange("p (n h) -> p n h", h=2)
                for h in range(2):
                    rows_ = slice(h * PAIR, (h + 1) * PAIR)
                    nc.vector.tensor_tensor(by_half[rows_, :, h], by_half[rows_, :, h], pair_lin[rows_],
                                            ALU.add).then_inc(lin_ready, 1)
                dve.wait_ge(lin_ready, (number + 1) * 2)
                nc.vector.tensor_tensor(lin_wide[:].rearrange("p (n b) -> p n b", b=BLOCK),
                                        lin_sum[:].unsqueeze(2).to_broadcast([P, GROUP, BLOCK]),
                                        col[:, SEL:SEL + P].rearrange("p (n b) -> p n b", b=BLOCK),
                                        ALU.mult).then_inc(lin_wide_ready, 1)
                dve.wait_ge(squares_ready, number + 1)
                nc.vector.tensor_reduce(sq_sum[:], x_sq[:, 0:QUADS].rearrange("p q b -> p b q"),
                                        AX.X, ALU.add).then_inc(sum_step, 1)
                dve.wait_ge(sum_step, number * 3 + 3)
                nc.vector.tensor_tensor(sq_sum[0:PAIR], sq_sum[0:PAIR],
                                        x_sq[0:PAIR, QUADS], ALU.add).then_inc(sq_sum_ready, 1)
                dve.wait_ge(sq_sum_ready, number + 1)
                dve.wait_ge(lin_wide_ready, number + 1)
                nc.vector.scalar_tensor_tensor(row_part[:], sq_sum[:], -0.5, lin_wide[:], ALU.mult, ALU.add
                                               ).then_inc(row_part_ready, 1)

            dve.wait_ge(dense_loaded, 16)
            dve.wait_ge(col_loaded, 16)
            with dve.Fori(0, GROUPS) as g:
                turn_group(g)
                sum_group(g)

        @block.tensor
        def _(pe):
            def layer(ps_, w, m, k, rhs, start, stop):
                return nc.tensor.matmul(ps_, w[0:rhs.shape[0], k, m * P:m * P + P], rhs,
                                        start=start, stop=stop, skip_group_check=True)

            def multiply_group(number):
                for i, k in enumerate(ORDER):
                    pe.wait_ge(w0_loaded[k], 16)
                    pe.wait_ge(x_ready, number * SLICES + i + 1)
                    n = TAIL if k == QUADS else P
                    for m in range(M1):
                        mm = layer(l0_out[m], w0_sb, m, k, x_t[0:n, k],
                                   start=(i == 0 and m % 2 == 0), stop=(i == SLICES - 1))
                        if i == SLICES - 1:
                            mm.then_inc(l0_done, 1)
                early = M1 // 2
                for k in range(early):
                    if k * W1_PIECES % M1 == 0:
                        pe.wait_ge(w1_loaded[k * W1_PIECES // M1], 16)
                    pe.wait_ge(h1_ready, number * M1 + k + 1)
                    for m in range(M2):
                        layer(l1_out[m], w1_sb, m, k, h1[:, k, :],
                              start=(k == 0 and m % 2 == 0), stop=False)
                for m in range(M2):
                    for k in range(early, M1):
                        if m == 0 and k * W1_PIECES % M1 == 0:
                            pe.wait_ge(w1_loaded[k * W1_PIECES // M1], 16)
                        if m == 0:
                            pe.wait_ge(h1_ready, number * M1 + k + 1)
                        mm = layer(l1_out[m], w1_sb, m, k, h1[:, k, :],
                                   start=False, stop=(k == M1 - 1))
                    mm.then_inc(l1_done, 1)
                pe.wait_ge(w2_loaded, 16)
                for k in range(M2):
                    pe.wait_ge(h2_ready, number * M2 + k + 1)
                    for m in range(M3):
                        mm = layer(l2_out[m], w2_sb, m, k, h2[:, k, :],
                                   start=(k == 0), stop=(k == M2 - 1))
                        if k == M2 - 1:
                            mm.then_inc(l2_done, 1)
                pe.wait_ge(emb_sum_ready, number + 1)
                nc.tensor.matmul(emb_sum_out, col[:, SEL:SEL + P], emb_sum[:],
                                 start=True, stop=True).then_inc(s_done, 1)
                pe.wait_ge(row_part_ready, number + 1)
                nc.tensor.matmul(logit_row, weight[:, 0:1], row_part[:], start=True, stop=False,
                                 skip_group_check=True)
                for k in range(M3):
                    pe.wait_ge(h3_ready, number * M3 + k + 1)
                    nc.tensor.matmul(logit_row, col[:, WOUT + k:WOUT + k + 1], h3[:, k, :],
                                     start=False, stop=False, skip_group_check=True)
                pe.wait_ge(s_sq_ready, number + 1)
                nc.tensor.matmul(logit_row, weight[:, 1:2], s_sq[:], start=False, stop=True,
                                 skip_group_check=True).then_inc(logit_done, 1)

            pe.wait_ge(col_loaded, 16)
            pe.wait_ge(weight_set, 2)
            with pe.Fori(0, GROUPS) as g:
                multiply_group(g)

        @block.scalar
        def _(act):
            def relu_layer(h, outs, per_bank, bias_at, number, done, ready):
                for m, ps_ in enumerate(outs):
                    act.wait_ge(done, number * len(outs) + m // per_bank * per_bank + per_bank)
                    nc.scalar.activation(h[:, m, :], ps_, ACT.Relu,
                                         bias=col[:, bias_at + m:bias_at + m + 1]).then_inc(ready, 1)

            def activate_group(number):
                relu_layer(h1, l0_out, 2, B0, number, l0_done, h1_ready)
                nc.scalar.activation(x_sq[:, 0:QUADS], x_t[:, 0:QUADS], ACT.Square)
                nc.scalar.activation(x_sq[0:PAIR, QUADS], x_t[0:PAIR, QUADS],
                                     ACT.Square).then_inc(squares_ready, 1)
                relu_layer(h2, l1_out, 2, B1, number, l1_done, h2_ready)
                relu_layer(h3, l2_out, 1, B2, number, l2_done, h3_ready)
                act.wait_ge(s_done, number + 1)
                nc.scalar.activation(s_sq[:], emb_sum_out, ACT.Square).then_inc(s_sq_ready, 1)
                act.wait_ge(logit_done, number + 1)
                nc.scalar.activation(probs[:, bass.ds(number * WIDTH, WIDTH)], logit_row, ACT.Sigmoid,
                                     bias=col[0:1, BOUT:BOUT + 1]).then_inc(probs_ready, 1)

            act.wait_ge(warm_set, 1)
            nc.scalar.activation(warm[:], warm[:], ACT.Sigmoid)
            act.wait_ge(col_loaded, 16)
            with act.Fori(0, GROUPS) as g:
                activate_group(g)


def kernel(r_x_dense, r_x_sparse, L0_rec_emb_tables, L0_rec_lin_tables, L0_rec_W0, L0_rec_b0,
           L0_rec_W1, L0_rec_b1, L0_rec_W2, L0_rec_b2, L0_rec_Wout, L0_rec_bout):
    import numpy as np
    import concourse.bacc as bacc
    from concourse.bass_utils import run_bass_kernel_spmd

    emb, lin = np.asarray(L0_rec_emb_tables), np.asarray(L0_rec_lin_tables)
    features, vocab, d = emb.shape
    batch = r_x_sparse.shape[0]
    per_quad = P // BLOCK
    quads = features // per_quad
    blocks = batch // BLOCK

    table = np.concatenate([emb, lin[:, :, None]], axis=2).reshape(features * vocab, d + 1)

    def by_gather(x):
        x = x.reshape(blocks, BLOCK, features)
        quad = x[:, :, :quads * per_quad].reshape(blocks, BLOCK, quads, per_quad)
        quad = quad.transpose(3, 1, 0, 2).reshape(P, blocks // 2, 2 * quads)
        pair = x[:, :, quads * per_quad:].reshape(blocks // 2, 2, BLOCK, features - quads * per_quad)
        pair = pair.transpose(1, 3, 2, 0).reshape(P, blocks // 2, 1)
        return np.concatenate([quad, pair], axis=2).reshape(P, -1)

    first_row = np.broadcast_to(np.arange(0, features * vocab, vocab, dtype=np.int32), (batch, features))
    slots = np.concatenate([by_gather(np.asarray(r_x_sparse)), by_gather(first_row)], axis=1).reshape(P, 2, -1)

    def in_columns(v):
        return np.asarray(v).reshape(-1, P).T

    bout = np.broadcast_to(np.asarray(L0_rec_bout).reshape(1, 1), (P, 1))
    sel = np.tile(np.eye(BLOCK, dtype=np.float32), (per_quad, per_quad))
    columns = np.concatenate([in_columns(L0_rec_b0), in_columns(L0_rec_b1), in_columns(L0_rec_b2),
                              in_columns(L0_rec_Wout), bout, sel], axis=1)
    arrays = {
        "table": table, "slots": slots, "w0": np.asarray(L0_rec_W0), "w1": np.asarray(L0_rec_W1),
        "w2": np.asarray(L0_rec_W2), "dense_t": np.asarray(r_x_dense).T, "columns": columns,
    }
    arrays = {k: np.ascontiguousarray(a) for k, a in arrays.items()}

    nc = bacc.Bacc("TRN2", target_bir_lowering=False, num_devices=1)
    args = [nc.dram_tensor(k, a.shape, mybir.dt.from_np(a.dtype), kind="ExternalInput").ap()
            for k, a in arrays.items()]
    out = nc.dram_tensor("out", (batch,), F32, kind="ExternalOutput").ap()
    deepfm(nc, *args, out)
    r = run_bass_kernel_spmd(nc, [arrays], core_ids=[0])
    return r.results[0]["out"]
```
